# Optimizing a Trainium2 kernel written in Bass

```python
import numpy as np
import jax
import jax.numpy as jnp

def _softmax(x, axis=-1):
    return jax.nn.softmax(x, axis=axis)

def _gelu(x):
    return jax.nn.gelu(x, approximate=True)

def _silu(x):
    return jax.nn.silu(x)

def _sigmoid(x):
    return jax.nn.sigmoid(x)

def _layernorm(x, axis=-1, eps=1e-05):
    m = jnp.mean(x, axis=axis, keepdims=True)
    v = jnp.var(x, axis=axis, keepdims=True)
    return (x - m) / jnp.sqrt(v + eps)

def _scatter_add(tgt, idx, src, axis=0):
    return tgt.at[idx].add(src)

def _segment_sum(src, seg, n):
    return jax.ops.segment_sum(src, seg, n)
kernel_name = 'mk_dlrm_tower_d1_rec_r8_c4a987'

def setup_inputs(seed: int=0):
    np.random.seed(seed)
    _w = jnp.asarray

    def _rec_inputs():
        import jax
        import jax.numpy as jnp
        _tk = jax.random.key(seed)
        ids = jnp.stack([jax.random.randint(jax.random.fold_in(_tk, 200 + f), (512,), 0, v, jnp.int32) for f, v in enumerate([1000, 1000, 1250, 12500, 1250, 12500, 125000, 1250, 1250, 12500, 1000, 1000, 1250, 12500, 12500, 12500, 12500, 1000, 1000, 12500, 1000, 1000, 1000, 1250, 1000, 1250])], axis=1)
        tbl_0 = 0.05 * jax.random.normal(jax.random.fold_in(_tk, 500 + 0), (1000, 128), jnp.float32)
        tbl_1 = 0.05 * jax.random.normal(jax.random.fold_in(_tk, 500 + 1), (1000, 128), jnp.float32)
        tbl_2 = 0.05 * jax.random.normal(jax.random.fold_in(_tk, 500 + 2), (1250, 128), jnp.float32)
        tbl_3 = 0.05 * jax.random.normal(jax.random.fold_in(_tk, 500 + 3), (12500, 128), jnp.float32)
        tbl_4 = 0.05 * jax.random.normal(jax.random.fold_in(_tk, 500 + 4), (1250, 128), jnp.float32)
        tbl_5 = 0.05 * jax.random.normal(jax.random.fold_in(_tk, 500 + 5), (12500, 128), jnp.float32)
        tbl_6 = 0.05 * jax.random.normal(jax.random.fold_in(_tk, 500 + 6), (125000, 128), jnp.float32)
        tbl_7 = 0.05 * jax.random.normal(jax.random.fold_in(_tk, 500 + 7), (1250, 128), jnp.float32)
        tbl_8 = 0.05 * jax.random.normal(jax.random.fold_in(_tk, 500 + 8), (1250, 128), jnp.float32)
        tbl_9 = 0.05 * jax.random.normal(jax.random.fold_in(_tk, 500 + 9), (12500, 128), jnp.float32)
        tbl_10 = 0.05 * jax.random.normal(jax.random.fold_in(_tk, 500 + 10), (1000, 128), jnp.float32)
        tbl_11 = 0.05 * jax.random.normal(jax.random.fold_in(_tk, 500 + 11), (1000, 128), jnp.float32)
        tbl_12 = 0.05 * jax.random.normal(jax.random.fold_in(_tk, 500 + 12), (1250, 128), jnp.float32)
        tbl_13 = 0.05 * jax.random.normal(jax.random.fold_in(_tk, 500 + 13), (12500, 128), jnp.float32)
        tbl_14 = 0.05 * jax.random.normal(jax.random.fold_in(_tk, 500 + 14), (12500, 128), jnp.float32)
        tbl_15 = 0.05 * jax.random.normal(jax.random.fold_in(_tk, 500 + 15), (12500, 128), jnp.float32)
        tbl_16 = 0.05 * jax.random.normal(jax.random.fold_in(_tk, 500 + 16), (12500, 128), jnp.float32)
        tbl_17 = 0.05 * jax.random.normal(jax.random.fold_in(_tk, 500 + 17), (1000, 128), jnp.float32)
        tbl_18 = 0.05 * jax.random.normal(jax.random.fold_in(_tk, 500 + 18), (1000, 128), jnp.float32)
        tbl_19 = 0.05 * jax.random.normal(jax.random.fold_in(_tk, 500 + 19), (12500, 128), jnp.float32)
        tbl_20 = 0.05 * jax.random.normal(jax.random.fold_in(_tk, 500 + 20), (1000, 128), jnp.float32)
        tbl_21 = 0.05 * jax.random.normal(jax.random.fold_in(_tk, 500 + 21), (1000, 128), jnp.float32)
        tbl_22 = 0.05 * jax.random.normal(jax.random.fold_in(_tk, 500 + 22), (1000, 128), jnp.float32)
        tbl_23 = 0.05 * jax.random.normal(jax.random.fold_in(_tk, 500 + 23), (1250, 128), jnp.float32)
        tbl_24 = 0.05 * jax.random.normal(jax.random.fold_in(_tk, 500 + 24), (1000, 128), jnp.float32)
        tbl_25 = 0.05 * jax.random.normal(jax.random.fold_in(_tk, 500 + 25), (1250, 128), jnp.float32)
        _rk = jax.random.fold_in(_tk, 7)
        r_dense_x = -0.000514642 + 1.00011 * jax.random.normal(jax.random.fold_in(_rk, 101), (512, 128), jnp.float32)
        W_top1 = 0.0456912 * jax.random.normal(jax.random.fold_in(_tk, 801), (479, 512), jnp.float32)
        W_top2 = 0.0441942 * jax.random.normal(jax.random.fold_in(_tk, 802), (512, 256), jnp.float32)
        W_top3 = 0.0625 * jax.random.normal(jax.random.fold_in(_tk, 803), (256, 1), jnp.float32)
        b_top1 = jnp.zeros((512,), jnp.float32)
        b_top2 = jnp.zeros((256,), jnp.float32)
        return (r_dense_x, ids, tbl_0, tbl_1, tbl_2, tbl_3, tbl_4, tbl_5, tbl_6, tbl_7, tbl_8, tbl_9, tbl_10, tbl_11, tbl_12, tbl_13, tbl_14, tbl_15, tbl_16, tbl_17, tbl_18, tbl_19, tbl_20, tbl_21, tbl_22, tbl_23, tbl_24, tbl_25, W_top1, b_top1, W_top2, b_top2, W_top3)
    r_dense_x, ids, tbl_0, tbl_1, tbl_2, tbl_3, tbl_4, tbl_5, tbl_6, tbl_7, tbl_8, tbl_9, tbl_10, tbl_11, tbl_12, tbl_13, tbl_14, tbl_15, tbl_16, tbl_17, tbl_18, tbl_19, tbl_20, tbl_21, tbl_22, tbl_23, tbl_24, tbl_25, W_top1, b_top1, W_top2, b_top2, W_top3 = _rec_inputs()

    def _L0_rec_setup():
        import jax, jax.numpy as jnp
        import numpy as np
        F = 26
        D = 128
        B = 2048
        _TRIU_I, _TRIU_J = np.triu_indices(F + 1, k=1)
        _TRIU_I = jnp.asarray(_TRIU_I)
        _TRIU_J = jnp.asarray(_TRIU_J)
        key = jax.random.key(seed)
        k1, k2 = jax.random.split(key)
        sparse_x = jax.random.normal(k1, (B, F, D), dtype=jnp.float32)
        dense_x = jax.random.normal(k2, (B, D), dtype=jnp.float32)
        return {'sparse_x': sparse_x, 'dense_x': dense_x}
    _L0_rec_all = _L0_rec_setup()
    _L0_rec_in = {k: v for k, v in _L0_rec_all.items() if k in ()}
    del _L0_rec_all
    return {'r_dense_x': r_dense_x, 'ids': ids, 'tbl_0': tbl_0, 'tbl_1': tbl_1, 'tbl_2': tbl_2, 'tbl_3': tbl_3, 'tbl_4': tbl_4, 'tbl_5': tbl_5, 'tbl_6': tbl_6, 'tbl_7': tbl_7, 'tbl_8': tbl_8, 'tbl_9': tbl_9, 'tbl_10': tbl_10, 'tbl_11': tbl_11, 'tbl_12': tbl_12, 'tbl_13': tbl_13, 'tbl_14': tbl_14, 'tbl_15': tbl_15, 'tbl_16': tbl_16, 'tbl_17': tbl_17, 'tbl_18': tbl_18, 'tbl_19': tbl_19, 'tbl_20': tbl_20, 'tbl_21': tbl_21, 'tbl_22': tbl_22, 'tbl_23': tbl_23, 'tbl_24': tbl_24, 'tbl_25': tbl_25, 'W_top1': W_top1, 'b_top1': b_top1, 'W_top2': W_top2, 'b_top2': b_top2, 'W_top3': W_top3}

def reference(r_dense_x, ids, tbl_0, tbl_1, tbl_2, tbl_3, tbl_4, tbl_5, tbl_6, tbl_7, tbl_8, tbl_9, tbl_10, tbl_11, tbl_12, tbl_13, tbl_14, tbl_15, tbl_16, tbl_17, tbl_18, tbl_19, tbl_20, tbl_21, tbl_22, tbl_23, tbl_24, tbl_25, W_top1, b_top1, W_top2, b_top2, W_top3):
    import jax
    import jax.numpy as jnp

    def _L0_rec_ref(sparse_x, dense_x):
        import jax, jax.numpy as jnp
        import numpy as np
        F = 26
        D = 128
        B = 2048
        _TRIU_I, _TRIU_J = np.triu_indices(F + 1, k=1)
        _TRIU_I = jnp.asarray(_TRIU_I)
        _TRIU_J = jnp.asarray(_TRIU_J)
        combined = jnp.concatenate([sparse_x, dense_x[:, None, :]], axis=1)
        interact = jnp.einsum('bfd,bgd->bfg', combined, combined)
        return interact[:, _TRIU_I, _TRIU_J]
    e = jnp.stack([tbl_0[ids[:, 0]], tbl_1[ids[:, 1]], tbl_2[ids[:, 2]], tbl_3[ids[:, 3]], tbl_4[ids[:, 4]], tbl_5[ids[:, 5]], tbl_6[ids[:, 6]], tbl_7[ids[:, 7]], tbl_8[ids[:, 8]], tbl_9[ids[:, 9]], tbl_10[ids[:, 10]], tbl_11[ids[:, 11]], tbl_12[ids[:, 12]], tbl_13[ids[:, 13]], tbl_14[ids[:, 14]], tbl_15[ids[:, 15]], tbl_16[ids[:, 16]], tbl_17[ids[:, 17]], tbl_18[ids[:, 18]], tbl_19[ids[:, 19]], tbl_20[ids[:, 20]], tbl_21[ids[:, 21]], tbl_22[ids[:, 22]], tbl_23[ids[:, 23]], tbl_24[ids[:, 24]], tbl_25[ids[:, 25]]], axis=1)
    z = _L0_rec_ref(e, r_dense_x)
    z = z.reshape(z.shape[0], -1)
    h = jnp.concatenate([z, r_dense_x], axis=1)
    h = jnp.maximum(h @ W_top1 + b_top1, 0.0)
    h = jnp.maximum(h @ W_top2 + b_top2, 0.0)
    y = h @ W_top3
    return y

_drawn_inputs = setup_inputs


def setup_inputs(seed=0):
    import zlib

    import numpy as np

    out = dict(_drawn_inputs(seed))
    spreads = {'b_top1': (0.0, 0.1), 'b_top2': (0.0, 0.1)}
    factors = {}
    for name, (base, spread) in spreads.items():
        noise = np.random.default_rng([zlib.crc32(name.encode()), seed]).standard_normal(out[name].shape)
        drawn = base * np.exp(spread * noise) if base else spread * noise
        out[name] = jnp.asarray(drawn.astype(out[name].dtype))
    for name, factor in factors.items():
        out[name] = (out[name] * factor).astype(out[name].dtype)
    return out
```

```python
import concourse.bass as bass
from concourse import mybir
from contextlib import ExitStack

P = 128


def dlrm_tower(nc, ids, dense, tables, w1, b1, w2, b2, w3, out):
    fp32 = mybir.dt.float32
    i32 = mybir.dt.int32
    ALU = mybir.AluOpType
    ACT = mybir.ActivationFunctionType

    batch, n_tables = ids.shape
    depth = dense.shape[1]
    assert depth == P
    tiles = batch // P
    feats = n_tables + 1
    hid1, hid2 = w2.shape
    n1, n2 = hid1 // P, hid2 // P

    QUAD = 32
    QUADS = P // QUAD
    cols = feats - 1
    share = [cols // QUADS + (q < cols % QUADS) for q in range(QUADS)]
    first = [sum(share[:q]) for q in range(QUADS)]
    n_z = max(share)
    z_rows = [QUAD * sum(s > c for s in share) for c in range(n_z)]
    pair_row = [i * (2 * feats - i - 1) // 2 for i in range(cols)]
    n_pairs = feats * cols // 2

    PER = 4
    lots = [range(f, min(f + PER, feats)) for f in range(0, feats, PER)]
    n_lots = len(lots)
    HALF = 16
    HALVES = QUAD // HALF
    assert HALF * cols <= 512

    ctx = ExitStack()
    with ctx:
        def sb(name, shape, dt=fp32):
            return ctx.enter_context(nc.sbuf_tensor(name, shape, dt))

        def pb(name, shape):
            return ctx.enter_context(nc.psum_tensor(name, shape, fp32))

        def sem(name):
            return ctx.enter_context(nc.semaphore(name))

        idx = sb("idx", [P, tiles, n_tables], i32)
        rows = sb("rows", [P, tiles, feats, depth])
        ident = sb("ident", [P, P])
        T = sb("T", [P, batch, QUAD])
        Z = sb("Z", [P, n_z, batch])
        W1z = sb("W1z", [P, n_z, hid1])
        W1x = sb("W1x", [P, hid1])
        W2 = sb("W2", [P, n1, hid2])
        n_small = n1 + n2 + n2
        small_rows = sb("small_rows", [n_small, P])
        small = sb("small", [P, n_small])
        B1 = small[:, 0:n1]
        B2 = small[:, n1:n1 + n2]
        W3 = small[:, n1 + n2:n_small]
        H1 = sb("H1", [P, n1, P])
        H2 = sb("H2", [P, n2, P])
        y = sb("y", [1, batch])

        pT = [pb(f"pT{i}", [P, PER * P]) for i in range(2)]
        pZ = [pb(f"pZ{i}", [P, HALVES, 512]) for i in range(2)]
        pH1 = pb("pH1", [P, n1, P])
        pH2 = pb("pH2", [P, n2 + 1, P])
        pY = pH2[0:1, n2, :]

        idx_in = sem("idx_in")
        dense_in = sem("dense_in")
        small_in = sem("small_in")
        small_turned = sem("small_turned")
        small_kept = sem("small_kept")
        w1_in = sem("w1_in")
        w2_in = sem("w2_in")
        rows_in = [[sem(f"rows_in_{t}_{m}") for m in range(n_lots)] for t in range(tiles)]
        ident_set = sem("ident_set")
        pads_zero = sem("pads_zero")
        w1_zero = sem("w1_zero")
        lot_turned = sem("lot_turned")
        lot_kept_v = sem("lot_kept_v")
        lot_kept_a = sem("lot_kept_a")
        products = sem("products")
        spread_v = sem("spread_v")
        spread_a = sem("spread_a")
        h1_sum = sem("h1_sum")
        h1_kept = sem("h1_kept")
        h2_sum = sem("h2_sum")
        h2_kept = sem("h2_kept")
        y_sum = sem("y_sum")
        y_kept = sem("y_kept")
        y_out = sem("y_out")

        def lot_number(t, m):
            return t * n_lots + m

        def wait_lot_kept(eng, n):
            eng.wait_ge(lot_kept_a if n % 2 else lot_kept_v, n // 2 + 1)

        def lot_views(t, m):
            n = lot_number(t, m)
            k = len(lots[m])
            src = pT[n % 2][:, 0:k * P].rearrange("d (f b) -> d f b", f=k)
            dst = T[:, t * P:(t + 1) * P, lots[m][0]:lots[m][0] + k].rearrange("d b f -> d f b")
            return dst, src

        def spread_views(t, j, q):
            i0, k = first[q], share[q]
            src = pZ[t % 2][QUAD * j:QUAD * (j + 1), :, 0:HALF * cols]
            src = src.rearrange("g h (s i) -> g h s i", i=cols)[:, :, :, i0:i0 + k]
            b0 = t * P + QUAD * j
            dst = Z[QUAD * q:QUAD * (q + 1), 0:k, b0:b0 + QUAD]
            return dst.rearrange("g i (h s) -> g h s i", h=HALVES), src

        SPREADS_V = [(j, q) for j in range(0, QUADS // 2) for q in range(QUADS)]
        SPREADS_A = [(j, q) for j in range(QUADS // 2, QUADS) for q in range(QUADS)]

        block = ctx.enter_context(nc.Block())

        @block.sync
        def _(sp):
            sp.dma_start(idx[:, :, :], ids.rearrange("(t p) f -> p t f", p=P)).then_inc(idx_in, 16)
            sp.dma_start(rows[:, :, n_tables, :], dense.rearrange("(t p) d -> p t d", p=P)).then_inc(dense_in, 16)
            sp.wait_ge(w1_zero, 1)
            for q in range(QUADS):
                for c in range(share[q]):
                    i = first[q] + c
                    k = feats - 1 - i
                    sp.dma_start(W1z[QUAD * q + i + 1:QUAD * q + feats, c, :],
                                 w1[pair_row[i]:pair_row[i] + k, :]).then_inc(w1_in, 16)
            sp.wait_ge(y_kept, tiles)
            sp.dma_start(out.rearrange("b o -> o b"), y[:, :]).then_inc(y_out, 16)
            sp.wait_ge(y_out, 16)

        @block.gpsimd
        def _(pool):
            nc.gpsimd.memset(ident[:, :], 0.0).then_inc(ident_set, 1)
            pool.wait_ge(ident_set, 1)
            nc.gpsimd.affine_select(out=ident[:, :], in_=ident[:, :], compare_op=ALU.not_equal, fill=1.0,
                                    base=0, pattern=[[-1, P]], channel_multiplier=1).then_inc(ident_set, 1)
            pool.wait_ge(idx_in, 16)
            for t in range(tiles):
                for m in range(n_lots):
                    for f in lots[m]:
                        if f < n_tables:
                            pool.indirect_dma_start(
                                out=rows[:, t, f, :], out_offset=None, in_=tables[f],
                                in_offset=bass.IndirectOffsetOnAxis(ap=idx[:, t, f:f + 1], axis=0),
                            ).then_inc(rows_in[t][m], 16)

        @block.vector
        def _(dve):
            nc.vector.memset(W1z[:, :, :], 0.0).then_inc(w1_zero, 1)
            nc.vector.memset(T[:, :, feats:QUAD], 0.0).then_inc(pads_zero, 1)

            dve.wait_ge(small_turned, 1)
            nc.vector.tensor_copy(small[:, :], pH2[:, 0, 0:n_small]).then_inc(small_kept, 1)

            def keep_lot(t, m):
                n = lot_number(t, m)
                if n % 2 == 0:
                    dve.wait_ge(lot_turned, n + 1)
                    nc.vector.tensor_copy(*lot_views(t, m)).then_inc(lot_kept_v, 1)

            def spread(t):
                dve.wait_ge(products, t + 1)
                for j, q in SPREADS_V:
                    last = nc.vector.tensor_copy(*spread_views(t, j, q))
                last.then_inc(spread_v, 1)

            def relu2(t):
                dve.wait_ge(h2_sum, t + 1)
                for n in range(n2):
                    last = nc.vector.tensor_scalar(H2[:, n, :], pH2[:, n, :], B2[:, n:n + 1], 0.0,
                                                   ALU.add, ALU.max)
                last.then_inc(h2_kept, 1)

            def keep_y(t):
                dve.wait_ge(y_sum, t + 1)
                nc.vector.tensor_copy(y[:, t * P:(t + 1) * P], pY).then_inc(y_kept, 1)

            for t in range(tiles + 1):
                for m in range(n_lots):
                    if t < tiles:
                        keep_lot(t, m)
                    if t > 0 and m == 3:
                        relu2(t - 1)
                    if t > 0 and m == 5:
                        keep_y(t - 1)
                if t < tiles:
                    spread(t)

        @block.scalar
        def _(act):
            act.dma_start(small_rows[0:n1, :], b1.rearrange("(c p) -> c p", p=P)).then_inc(small_in, 16)
            act.dma_start(small_rows[n1:n1 + n2, :], b2.rearrange("(c p) -> c p", p=P)).then_inc(small_in, 16)
            act.dma_start(small_rows[n1 + n2:n_small, :],
                          w3.rearrange("(c p) o -> c (p o)", p=P)).then_inc(small_in, 16)
            act.dma_start(W1x[:, :], w1[n_pairs:n_pairs + depth, :]).then_inc(w2_in, 16)
            act.dma_start(W2[:, :, :], w2.rearrange("(c p) n -> p c n", p=P)).then_inc(w2_in, 16)

            def keep_lot(t, m):
                n = lot_number(t, m)
                if n % 2 == 1:
                    act.wait_ge(lot_turned, n + 1)
                    nc.scalar.copy(*lot_views(t, m)).then_inc(lot_kept_a, 1)

            def spread(t):
                act.wait_ge(products, t + 1)
                for j, q in SPREADS_A:
                    last = nc.scalar.copy(*spread_views(t, j, q))
                last.then_inc(spread_a, 1)

            def relu1(t):
                act.wait_ge(h1_sum, t + 1)
                if t == 0:
                    act.wait_ge(small_kept, 1)
                for n in range(n1):
                    last = nc.scalar.activation(H1[:, n, :], pH1[:, n, :], ACT.Relu, bias=B1[:, n:n + 1])
                last.then_inc(h1_kept, 1)

            for t in range(tiles + 1):
                for m in range(n_lots):
                    if t < tiles:
                        keep_lot(t, m)
                    if t > 0 and m == 1:
                        relu1(t - 1)
                if t < tiles:
                    spread(t)

        @block.tensor
        def _(pe):
            pe.wait_ge(ident_set, 2)
            pe.wait_ge(small_in, 48)
            nc.tensor.transpose(pH2[:, 0, 0:n_small], small_rows[:, :],
                                ident[0:n_small, 0:n_small]).then_inc(small_turned, 1)

            def turn_lot(t, m):
                n = lot_number(t, m)
                if n >= 2:
                    wait_lot_kept(pe, n - 2)
                tables_in = sum(f < n_tables for f in lots[m])
                pe.wait_ge(rows_in[t][m], 16 * tables_in)
                if n_tables in lots[m] and t == 0:
                    pe.wait_ge(dense_in, 16)
                for s, f in enumerate(lots[m]):
                    last = nc.tensor.transpose(pT[n % 2][:, s * P:(s + 1) * P], rows[:, t, f, :], ident[:, :])
                last.then_inc(lot_turned, 1)

            def interact(t):
                if t == 0:
                    pe.wait_ge(pads_zero, 1)
                if t >= 2:
                    pe.wait_ge(spread_v, t - 1)
                    pe.wait_ge(spread_a, t - 1)
                wait_lot_kept(pe, lot_number(t, n_lots - 1))
                wait_lot_kept(pe, lot_number(t, n_lots - 2))
                for s in range(QUAD):
                    for j in range(QUADS):
                        b = t * P + QUAD * j + s
                        c0 = (s % HALF) * cols
                        last = nc.tensor.matmul(
                            pZ[t % 2][QUAD * j:QUAD * (j + 1), s // HALF, c0:c0 + cols],
                            T[:, b, :], T[:, b, 0:cols], start=True, stop=True)
                last.then_inc(products, 1)

            def layer1(t):
                if t == 0:
                    pe.wait_ge(w1_in, 16 * cols)
                    pe.wait_ge(w2_in, 32)
                else:
                    pe.wait_ge(h1_kept, t)
                pe.wait_ge(spread_v, t + 1)
                pe.wait_ge(spread_a, t + 1)
                bs = slice(t * P, (t + 1) * P)
                for n in range(n1):
                    ns = slice(n * P, (n + 1) * P)
                    nc.tensor.matmul(pH1[:, n, :], W1x[:, ns], T[:, bs, feats - 1], start=True, stop=False)
                    for c in range(n_z):
                        k = z_rows[c]
                        last = nc.tensor.matmul(pH1[:, n, :], W1z[0:k, c, ns], Z[0:k, c, bs],
                                                start=False, stop=c == n_z - 1)
                last.then_inc(h1_sum, 1)

            def layer2(t):
                pe.wait_ge(h1_kept, t + 1)
                if t == 0:
                    pe.wait_ge(small_kept, 1)
                else:
                    pe.wait_ge(y_kept, t)
                for n in range(n2):
                    for c in range(n1):
                        last = nc.tensor.matmul(pH2[:, n, :], W2[:, c, n * P:(n + 1) * P], H1[:, c, :],
                                                start=c == 0, stop=c == n1 - 1)
                last.then_inc(h2_sum, 1)

            def layer3(t):
                pe.wait_ge(h2_kept, t + 1)
                for c in range(n2):
                    last = nc.tensor.matmul(pY, W3[:, c:c + 1], H2[:, c, :], start=c == 0, stop=c == n2 - 1)
                last.then_inc(y_sum, 1)

            for t in range(tiles + 1):
                for m in range(n_lots):
                    if t < tiles:
                        turn_lot(t, m)
                    if t > 0 and m == 1:
                        layer1(t - 1)
                    if t > 0 and m == 3:
                        layer2(t - 1)
                    if t > 0 and m == 5:
                        layer3(t - 1)
                if t < tiles:
                    interact(t)


def kernel(**inputs):
    import numpy as np
    import concourse.bacc as bacc
    from concourse import mybir as mb
    from concourse.bass_utils import run_bass_kernel_spmd

    nc = bacc.Bacc("TRN2", target_bir_lowering=False, num_devices=1)
    arrays, aps = {}, {}
    for name, value in inputs.items():
        a = np.ascontiguousarray(value)
        arrays[f"in_{name}"] = a
        aps[name] = nc.dram_tensor(f"in_{name}", a.shape, mb.dt.from_np(a.dtype), kind="ExternalInput").ap()
    batch, n_tables = inputs["ids"].shape
    out = nc.dram_tensor("out", (batch, 1), mb.dt.float32, kind="ExternalOutput").ap()
    dlrm_tower(nc, aps["ids"], aps["r_dense_x"], [aps[f"tbl_{f}"] for f in range(n_tables)],
               aps["W_top1"], aps["b_top1"], aps["W_top2"], aps["b_top2"], aps["W_top3"], out)
    result = run_bass_kernel_spmd(nc, [arrays], core_ids=[0])
    return result.results[0]["out"]
```

```python
import concourse.bass as bass
from concourse import mybir
from contextlib import ExitStack

P = 128
LOOKUPS = 8


def dlrm_tower(nc, ids, dense, tables, w1, b1, w2, b2, w3, out):
    fp32 = mybir.dt.float32
    fp32r = mybir.dt.float32r
    fp16 = mybir.dt.float16
    i32 = mybir.dt.int32
    ALU = mybir.AluOpType
    ACT = mybir.ActivationFunctionType

    batch, n_tables = ids.shape
    depth = dense.shape[1]
    assert depth == P
    tiles = batch // P
    feats = n_tables + 1
    hid1, hid2 = w2.shape
    n1, n2 = hid1 // P, hid2 // P

    QUAD = 32
    QUADS = P // QUAD
    cols = feats - 1
    share = [cols // QUADS + (q < cols % QUADS) for q in range(QUADS)]
    first = [sum(share[:q]) for q in range(QUADS)]
    n_z = max(share)
    z_rows = [QUAD * sum(s > c for s in share) for c in range(n_z)]
    pair_row = [i * (2 * feats - i - 1) // 2 for i in range(cols + 1)]
    n_pairs = feats * cols // 2

    sizes = [table.shape[0] for table in tables]
    looked = sorted(sorted(range(n_tables), key=lambda f: sizes[f])[:LOOKUPS])
    assert max(sizes[f] for f in looked) <= 2048
    whole = [sizes[f] // P for f in looked]
    rest = [sizes[f] % P for f in looked]
    assert all(rest)
    chunks = [w + 1 for w in whole]
    max_chunks = max(chunks)
    widths = sorted(set(whole))
    RING = 8

    gathered = [f for f in range(n_tables) if f not in looked]
    PER = 4
    order = [n_tables] + gathered
    lots = [order[k:k + PER] for k in range(0, len(order), PER)]
    n_lots = len(lots)
    HALF = 16
    HALVES = QUAD // HALF
    assert HALF * cols <= 512

    ctx = ExitStack()
    with ctx:
        def sb(name, shape, dt=fp32):
            return ctx.enter_context(nc.sbuf_tensor(name, shape, dt))

        def pb(name, shape):
            return ctx.enter_context(nc.psum_tensor(name, shape, fp32))

        def sem(name):
            return ctx.enter_context(nc.semaphore(name))

        idx = sb("idx", [P, tiles, n_tables], i32)
        ids16 = sb("ids16", [P, tiles, n_tables], fp16)
        ident16 = sb("ident16", [P, P], fp16)
        table_rows = sb("table_rows", [P, 2, max_chunks, depth])
        table_hi = sb("table_hi", [P, 2, max_chunks, depth], fp32r)
        table_lo = sb("table_lo", [P, 2, max_chunks, depth], fp32r)
        row_of = [sb(f"row_of_{w}", [P, w + 1]) for w in widths]
        id_rows = sb("id_rows", [P, 2, batch])
        hot = sb("hot", [P, RING, batch], fp32r)
        rows = sb("rows", [P, tiles, len(order), depth])
        ident = sb("ident", [P, P])
        zero = sb("zero", [P, 1])
        T = sb("T", [P, batch, QUAD])
        Z = sb("Z", [P, n_z, batch])
        W1z = sb("W1z", [P, n_z, hid1])
        W1x = sb("W1x", [P, hid1])
        W2 = sb("W2", [P, n1, hid2])
        n_small = n1 + n2 + n2
        small_rows = sb("small_rows", [n_small, P])
        small = sb("small", [P, n_small])
        B1 = small[:, 0:n1]
        B2 = small[:, n1:n1 + n2]
        W3 = small[:, n1 + n2:n_small]
        H1 = sb("H1", [P, n1, P])
        H2 = sb("H2", [P, n2, P])
        y = sb("y", [1, batch])

        pT = [pb(f"pT{i}", [P, PER * P]) for i in range(2)]
        pZ = [pb(f"pZ{i}", [P, HALVES, 512]) for i in range(2)]
        pH1 = pb("pH1", [P, n1, P])
        pH2 = pb("pH2", [P, n2 + 1, P])
        pY = pH2[0:1, n2, :]

        idx_in = sem("idx_in")
        dense_in = sem("dense_in")
        table_in = [sem(f"table_in_{i}") for i in range(2)]
        ids16_made = sem("ids16_made")
        ids_spread = sem("ids_spread")
        ids_kept = sem("ids_kept")
        hi_made = sem("hi_made")
        lo_made = sem("lo_made")
        hot_made = sem("hot_made")
        hot_used = sem("hot_used")
        looked_kept = sem("looked_kept")
        small_in = sem("small_in")
        small_turned = sem("small_turned")
        small_kept = sem("small_kept")
        w1_in = sem("w1_in")
        w2_in = sem("w2_in")
        rows_in = [[sem(f"rows_in_{t}_{m}") for m in range(n_lots)] for t in range(tiles)]
        ident_set = sem("ident_set")
        ident16_set = sem("ident16_set")
        row_of_set = sem("row_of_set")
        zero_set = sem("zero_set")
        pads_zero = sem("pads_zero")
        w1_zero = sem("w1_zero")
        lot_turned = sem("lot_turned")
        lot_kept_v = sem("lot_kept_v")
        lot_kept_a = sem("lot_kept_a")
        products = sem("products")
        spread_v = sem("spread_v")
        spread_a = sem("spread_a")
        h1_sum = sem("h1_sum")
        h1_kept = sem("h1_kept")
        h2_sum = sem("h2_sum")
        h2_kept = sem("h2_kept")
        y_sum = sem("y_sum")
        y_kept = sem("y_kept")
        y_out = sem("y_out")

        def lot_number(t, m):
            return t * n_lots + m

        def by_act(t, m):
            return t == 0 or m % 2 == 1

        def wait_lot_kept(eng, t, m):
            before = [(u, k) for u in range(t + 1) for k in range(n_lots) if (u, k) <= (t, m)]
            count = sum(by_act(u, k) == by_act(t, m) for u, k in before)
            eng.wait_ge(lot_kept_a if by_act(t, m) else lot_kept_v, count)

        def lot_copies(t, m):
            lot = lots[m]
            starts = [s for s, f in enumerate(lot) if s == 0 or f != lot[s - 1] + 1]
            for s0, s1 in zip(starts, starts[1:] + [len(lot)]):
                src = pT[lot_number(t, m) % 2][:, s0 * P:s1 * P].rearrange("d (f b) -> d f b", f=s1 - s0)
                dst = T[:, t * P:(t + 1) * P, lot[s0]:lot[s0] + s1 - s0].rearrange("d b f -> d f b")
                yield dst, src

        def spread_views(t, h, j, q):
            i0, k = first[q], share[q]
            src = pZ[t % 2][QUAD * j:QUAD * (j + 1), h, 0:HALF * cols]
            src = src.rearrange("g (s i) -> g s i", i=cols)[:, :, i0:i0 + k]
            b0 = t * P + QUAD * j + HALF * h
            return Z[QUAD * q:QUAD * (q + 1), 0:k, b0:b0 + HALF].rearrange("g i s -> g s i"), src

        LOT_LAG = 2
        LOTS_A = range(0, n_lots - 2)
        LOTS_B = range(n_lots - 2, n_lots)

        SPREADS_V = [(j, q) for j in range(0, QUADS // 2) for q in range(QUADS)]
        SPREADS_A = [(j, q) for j in range(QUADS // 2, QUADS) for q in range(QUADS)]

        block = ctx.enter_context(nc.Block())

        @block.sync
        def _(sp):
            sp.dma_start(idx[:, :, :], ids.rearrange("(t p) f -> p t f", p=P)).then_inc(idx_in, 16)

            def load_table(k):
                if k >= 2:
                    sp.wait_ge(hi_made, k - 1)
                    sp.wait_ge(lo_made, k - 1)
                table, w, n = tables[looked[k]], whole[k], whole[k] * P
                sp.dma_start(table_rows[:, k % 2, 0:w, :],
                             table[0:n, :].rearrange("(p c) d -> p c d", c=w)).then_inc(table_in[k % 2], 16)
                sp.dma_start(table_rows[0:rest[k], k % 2, w, :],
                             table[n:n + rest[k], :]).then_inc(table_in[k % 2], 16)

            def load_w1(i):
                q = max(q for q in range(QUADS) if first[q] <= i)
                sp.dma_start(W1z[QUAD * q + i + 1:QUAD * q + feats, i - first[q], :],
                             w1[pair_row[i]:pair_row[i + 1], :]).then_inc(w1_in, 16)

            load_table(0)
            load_table(1)
            sp.dma_start(rows[:, :, 0, :], dense.rearrange("(t p) d -> p t d", p=P)).then_inc(dense_in, 16)
            sp.wait_ge(w1_zero, 1)
            w1_lot = -(-cols // (LOOKUPS - 1))
            for k in range(1, LOOKUPS):
                for i in range(w1_lot * (k - 1), min(w1_lot * k, cols)):
                    load_w1(i)
                if k + 1 < LOOKUPS:
                    load_table(k + 1)
            sp.wait_ge(y_kept, tiles)
            sp.dma_start(out.rearrange("b o -> o b"), y[:, :]).then_inc(y_out, 16)
            sp.wait_ge(y_out, 16)

        @block.gpsimd
        def _(pool):
            nc.gpsimd.memset(ident[:, :], 0.0).then_inc(ident_set, 1)
            pool.wait_ge(ident_set, 1)
            nc.gpsimd.affine_select(out=ident[:, :], in_=ident[:, :], compare_op=ALU.not_equal, fill=1.0,
                                    base=0, pattern=[[-1, P]], channel_multiplier=1).then_inc(ident_set, 1)
            for tile_, w in zip(row_of, widths):
                nc.gpsimd.iota(tile_[:, 0:w], pattern=[[1, w]], base=0, channel_multiplier=w,
                               allow_small_or_imprecise_dtypes=True).then_inc(row_of_set, 1)
                nc.gpsimd.iota(tile_[:, w:w + 1], pattern=[[1, 1]], base=w * P, channel_multiplier=1,
                               allow_small_or_imprecise_dtypes=True).then_inc(row_of_set, 1)
            pool.wait_ge(idx_in, 16)
            for t in range(tiles):
                for m in range(n_lots):
                    for f in lots[m]:
                        if f < n_tables:
                            pool.indirect_dma_start(
                                out=rows[:, t, order.index(f), :], out_offset=None, in_=tables[f],
                                in_offset=bass.IndirectOffsetOnAxis(ap=idx[:, t, f:f + 1], axis=0),
                            ).then_inc(rows_in[t][m], 16)

        @block.vector
        def _(dve):
            nc.vector.memset(zero[:, :], 0.0).then_inc(zero_set, 1)
            dve.wait_ge(idx_in, 16)
            nc.vector.tensor_copy(ids16[:, :, :], idx[:, :, :]).then_inc(ids16_made, 1)
            dve.wait_ge(ident_set, 2)
            nc.vector.tensor_copy(ident16[:, :], ident[:, :]).then_inc(ident16_set, 1)

            def make_lo(k):
                dve.wait_ge(hi_made, k + 1)
                w, part = whole[k], k % 2
                nc.vector.tensor_tensor(table_lo[:, part, 0:w, :], table_rows[:, part, 0:w, :],
                                        table_hi[:, part, 0:w, :], ALU.subtract)
                nc.vector.tensor_tensor(table_lo[0:rest[k], part, w, :], table_rows[0:rest[k], part, w, :],
                                        table_hi[0:rest[k], part, w, :], ALU.subtract).then_inc(lo_made, 1)

            def make_hot(k):
                dve.wait_ge(ids_kept, k + 1)
                if k == 0:
                    dve.wait_ge(row_of_set, 2 * len(widths))
                of = row_of[widths.index(whole[k])]
                for c in range(chunks[k]):
                    n = sum(chunks[:k]) + c
                    if n >= RING:
                        dve.wait_ge(hot_used, n - RING + 1)
                    nc.vector.tensor_scalar(hot[:, n % RING, :], id_rows[:, k % 2, :], of[:, c:c + 1], None,
                                            ALU.is_equal).then_inc(hot_made, 1)

            def keep_lot(t, m):
                if not by_act(t, m):
                    dve.wait_ge(lot_turned, lot_number(t, m) + 1)
                    for to, of in lot_copies(t, m):
                        last = nc.vector.tensor_copy(to, of)
                    last.then_inc(lot_kept_v, 1)

            def spread(t):
                for h in range(HALVES):
                    dve.wait_ge(products, HALVES * t + h + 1)
                    for j, q in SPREADS_V:
                        last = nc.vector.tensor_copy(*spread_views(t, h, j, q))
                    last.then_inc(spread_v, 1)

            def relu2(t):
                dve.wait_ge(h2_sum, t + 1)
                for n in range(n2):
                    last = nc.vector.tensor_scalar(H2[:, n, :], pH2[:, n, :], B2[:, n:n + 1], 0.0,
                                                   ALU.add, ALU.max)
                last.then_inc(h2_kept, 1)

            def keep_y(t):
                dve.wait_ge(y_sum, t + 1)
                nc.vector.tensor_copy(y[:, t * P:(t + 1) * P], pY).then_inc(y_kept, 1)

            for k in range(LOOKUPS):
                make_lo(k)
                make_hot(k)
                if k == 1:
                    dve.wait_ge(small_turned, 1)
                    nc.vector.tensor_copy(small[:, :], pH2[:, 0, 0:n_small]).then_inc(small_kept, 1)
            spread(0)
            for t in range(tiles):
                if t > 0:
                    relu2(t - 1)
                if t + 1 < tiles:
                    for m in range(n_lots):
                        keep_lot(t + 1, m)
                if t > 0:
                    keep_y(t - 1)
                if t + 1 < tiles:
                    spread(t + 1)
            relu2(tiles - 1)
            keep_y(tiles - 1)

        @block.scalar
        def _(act):
            act.dma_start(small_rows[0:n1, :], b1.rearrange("(c p) -> c p", p=P)).then_inc(small_in, 16)
            act.dma_start(small_rows[n1:n1 + n2, :], b2.rearrange("(c p) -> c p", p=P)).then_inc(small_in, 16)
            act.dma_start(small_rows[n1 + n2:n_small, :],
                          w3.rearrange("(c p) o -> c (p o)", p=P)).then_inc(small_in, 16)
            act.dma_start(W1x[:, :], w1[n_pairs:n_pairs + depth, :]).then_inc(w2_in, 16)
            act.dma_start(W2[:, :, :], w2.rearrange("(c p) n -> p c n", p=P)).then_inc(w2_in, 16)

            def keep_ids(k):
                act.wait_ge(ids_spread, k + 1)
                if k >= 2:
                    act.wait_ge(hot_made, sum(chunks[:k - 1]))
                nc.scalar.copy(id_rows[:, k % 2, :], pZ[1][:, k % 2, :]).then_inc(ids_kept, 1)

            def make_hi(k):
                act.wait_ge(table_in[k % 2], 32 * (k // 2 + 1))
                if k >= 2:
                    act.wait_ge(hot_used, sum(chunks[:k - 1]))
                w, part = whole[k], k % 2
                nc.scalar.copy(table_hi[:, part, 0:w, :], table_rows[:, part, 0:w, :])
                nc.scalar.copy(table_hi[0:rest[k], part, w, :],
                               table_rows[0:rest[k], part, w, :]).then_inc(hi_made, 1)

            def keep_looked(k):
                act.wait_ge(hot_used, sum(chunks[:k + 1]))
                nc.scalar.copy(T[:, :, looked[k]], pZ[0][:, k % 2, :]).then_inc(looked_kept, 1)

            def keep_lot(t, m):
                if by_act(t, m):
                    act.wait_ge(lot_turned, lot_number(t, m) + 1)
                    for to, of in lot_copies(t, m):
                        last = nc.scalar.copy(to, of)
                    last.then_inc(lot_kept_a, 1)

            def spread(t):
                for h in range(HALVES):
                    act.wait_ge(products, HALVES * t + h + 1)
                    for j, q in SPREADS_A:
                        last = nc.scalar.copy(*spread_views(t, h, j, q))
                    last.then_inc(spread_a, 1)

            def relu1(t):
                act.wait_ge(h1_sum, t + 1)
                if t == 0:
                    act.wait_ge(small_kept, 1)
                for n in range(n1):
                    last = nc.scalar.activation(H1[:, n, :], pH1[:, n, :], ACT.Relu, bias=B1[:, n:n + 1])
                last.then_inc(h1_kept, 1)

            make_hi(0)
            keep_ids(0)
            make_hi(1)
            keep_ids(1)
            act.wait_ge(zero_set, 1)
            nc.scalar.copy(W1z[:, :, :].rearrange("p c n -> p (c n)"),
                           zero[:, :].broadcast_to((P, n_z * hid1))).then_inc(w1_zero, 1)
            for k in range(LOOKUPS):
                if 1 <= k < LOOKUPS - 1:
                    keep_ids(k + 1)
                    make_hi(k + 1)
                if k == LOOKUPS - 1:
                    nc.scalar.copy(T[:, :, feats:QUAD],
                                   zero[:, :].unsqueeze(2).broadcast_to((P, batch, QUAD - feats))).then_inc(pads_zero, 1)
                if 0 <= k - LOT_LAG < n_lots:
                    keep_lot(0, k - LOT_LAG)
                keep_looked(k)
            for m in range(LOOKUPS - LOT_LAG, n_lots):
                keep_lot(0, m)
            spread(0)
            for t in range(tiles):
                if t + 1 < tiles:
                    for m in range(n_lots):
                        keep_lot(t + 1, m)
                relu1(t)
                if t + 1 < tiles:
                    spread(t + 1)

        @block.tensor
        def _(pe):
            def turn_small():
                pe.wait_ge(ident_set, 2)
                pe.wait_ge(small_in, 48)
                nc.tensor.transpose(pH2[:, 0, 0:n_small], small_rows[:, :],
                                    ident[0:n_small, 0:n_small]).then_inc(small_turned, 1)

            def spread_ids(k):
                if k == 0:
                    pe.wait_ge(ids16_made, 1)
                    pe.wait_ge(ident16_set, 1)
                if k >= 2:
                    pe.wait_ge(ids_kept, k - 1)
                f = looked[k]
                for t in range(tiles):
                    last = nc.tensor.matmul(pZ[1][:, k % 2, t * P:(t + 1) * P],
                                            ids16[:, t, f:f + 1].broadcast_to((P, P)), ident16[:, :],
                                            start=True, stop=True)
                last.then_inc(ids_spread, 1)

            def look_up(k):
                if k >= 2:
                    pe.wait_ge(looked_kept, k - 1)
                pe.wait_ge(lo_made, k + 1)
                for c in range(chunks[k]):
                    n = sum(chunks[:k]) + c
                    r = P if c < whole[k] else rest[k]
                    pe.wait_ge(hot_made, n + 1)
                    nc.tensor.matmul(pZ[0][:, k % 2, :], table_hi[0:r, k % 2, c, :], hot[0:r, n % RING, :],
                                     start=c == 0, stop=False)
                    nc.tensor.matmul(pZ[0][:, k % 2, :], table_lo[0:r, k % 2, c, :], hot[0:r, n % RING, :],
                                     start=False, stop=c == whole[k]).then_inc(hot_used, 1)

            def turn_lot(t, m):
                n = lot_number(t, m)
                if n >= 2:
                    wait_lot_kept(pe, (n - 2) // n_lots, (n - 2) % n_lots)
                if n_tables in lots[m] and t == 0:
                    pe.wait_ge(ident_set, 2)
                    pe.wait_ge(dense_in, 16)
                pe.wait_ge(rows_in[t][m], 16 * sum(f < n_tables for f in lots[m]))
                for s, f in enumerate(lots[m]):
                    last = nc.tensor.transpose(pT[n % 2][:, s * P:(s + 1) * P],
                                               rows[:, t, order.index(f), :], ident[:, :])
                last.then_inc(lot_turned, 1)

            def interact(t):
                if t == 0:
                    pe.wait_ge(pads_zero, 1)
                    pe.wait_ge(looked_kept, LOOKUPS)
                if t >= 2:
                    pe.wait_ge(spread_v, HALVES * (t - 1))
                    pe.wait_ge(spread_a, HALVES * (t - 1))
                wait_lot_kept(pe, t, n_lots - 2)
                wait_lot_kept(pe, t, n_lots - 1)
                for s in range(QUAD):
                    for j in range(QUADS):
                        b = t * P + QUAD * j + s
                        c0 = (s % HALF) * cols
                        last = nc.tensor.matmul(
                            pZ[t % 2][QUAD * j:QUAD * (j + 1), s // HALF, c0:c0 + cols],
                            T[:, b, :], T[:, b, 0:cols], start=True, stop=True)
                    if s % HALF == HALF - 1:
                        last.then_inc(products, 1)

            def layer1(t, units):
                if units[0] == 0:
                    if t == 0:
                        pe.wait_ge(w1_in, 16 * cols)
                        pe.wait_ge(w2_in, 32)
                    else:
                        pe.wait_ge(h1_kept, t)
                    pe.wait_ge(spread_v, HALVES * (t + 1))
                    pe.wait_ge(spread_a, HALVES * (t + 1))
                bs = slice(t * P, (t + 1) * P)
                for n in units:
                    ns = slice(n * P, (n + 1) * P)
                    nc.tensor.matmul(pH1[:, n, :], W1x[:, ns], T[:, bs, feats - 1], start=True, stop=False)
                    for c in range(n_z):
                        k = z_rows[c]
                        last = nc.tensor.matmul(pH1[:, n, :], W1z[0:k, c, ns], Z[0:k, c, bs],
                                                start=False, stop=c == n_z - 1)
                if units[-1] == n1 - 1:
                    last.then_inc(h1_sum, 1)

            def layer2(t):
                pe.wait_ge(h1_kept, t + 1)
                if t == 0:
                    pe.wait_ge(small_kept, 1)
                else:
                    pe.wait_ge(y_kept, t)
                for n in range(n2):
                    for c in range(n1):
                        last = nc.tensor.matmul(pH2[:, n, :], W2[:, c, n * P:(n + 1) * P], H1[:, c, :],
                                                start=c == 0, stop=c == n1 - 1)
                last.then_inc(h2_sum, 1)

            def layer3(t):
                pe.wait_ge(h2_kept, t + 1)
                for c in range(n2):
                    last = nc.tensor.matmul(pY, W3[:, c:c + 1], H2[:, c, :], start=c == 0, stop=c == n2 - 1)
                last.then_inc(y_sum, 1)

            spread_ids(0)
            turn_small()
            for k in range(LOOKUPS):
                if k + 1 < LOOKUPS:
                    spread_ids(k + 1)
                look_up(k)
                if 0 <= k - LOT_LAG < n_lots:
                    turn_lot(0, k - LOT_LAG)
            for m in range(LOOKUPS - LOT_LAG, n_lots):
                turn_lot(0, m)
            interact(0)
            for t in range(tiles):
                if t > 0:
                    layer2(t - 1)
                if t + 1 < tiles:
                    for m in LOTS_A:
                        turn_lot(t + 1, m)
                layer1(t, range(0, n1 - 1))
                if t + 1 < tiles:
                    for m in LOTS_B:
                        turn_lot(t + 1, m)
                layer1(t, range(n1 - 1, n1))
                if t > 0:
                    layer3(t - 1)
                if t + 1 < tiles:
                    interact(t + 1)
            layer2(tiles - 1)
            layer3(tiles - 1)


def kernel(**inputs):
    import numpy as np
    import concourse.bacc as bacc
    from concourse import mybir as mb
    from concourse.bass_utils import run_bass_kernel_spmd

    nc = bacc.Bacc("TRN2", target_bir_lowering=False, num_devices=1)
    arrays, aps = {}, {}
    for name, value in inputs.items():
        a = np.ascontiguousarray(value)
        arrays[f"in_{name}"] = a
        aps[name] = nc.dram_tensor(f"in_{name}", a.shape, mb.dt.from_np(a.dtype), kind="ExternalInput").ap()
    batch, n_tables = inputs["ids"].shape
    out = nc.dram_tensor("out", (batch, 1), mb.dt.float32, kind="ExternalOutput").ap()
    dlrm_tower(nc, aps["ids"], aps["r_dense_x"], [aps[f"tbl_{f}"] for f in range(n_tables)],
               aps["W_top1"], aps["b_top1"], aps["W_top2"], aps["b_top2"], aps["W_top3"], out)
    result = run_bass_kernel_spmd(nc, [arrays], core_ids=[0])
    return result.results[0]["out"]
```

```python
import concourse.bass as bass
from concourse import mybir
from contextlib import ExitStack

P = 128
LOOKUPS = 8
LATE = 1


def dlrm_tower(nc, ids, dense, tables, w1, b1, w2, b2, w3, out):
    fp32 = mybir.dt.float32
    fp32r = mybir.dt.float32r
    fp16 = mybir.dt.float16
    i32 = mybir.dt.int32
    ALU = mybir.AluOpType
    ACT = mybir.ActivationFunctionType

    batch, n_tables = ids.shape
    depth = dense.shape[1]
    assert depth == P
    tiles = batch // P
    feats = n_tables + 1
    hid1, hid2 = w2.shape
    n1, n2 = hid1 // P, hid2 // P

    QUAD = 32
    QUADS = P // QUAD
    DUPS = 2
    slots = DUPS + feats
    cols = feats - 1
    width = DUPS + cols
    own = cols - DUPS
    share = [own // QUADS + (q < own % QUADS) for q in range(QUADS)]
    first = [sum(share[:q]) for q in range(QUADS)]
    n_z = max(share)
    z_rows = [QUAD * sum(s > c for s in share) for c in range(n_z)]

    def pair(i, g):
        return i * (2 * feats - i - 1) // 2 + g - i - 1

    n_pairs = feats * (feats - 1) // 2

    sizes = [table.shape[0] for table in tables]
    looked = sorted(sorted(range(n_tables), key=lambda f: sizes[f])[:LOOKUPS])
    assert max(sizes[f] for f in looked) <= 2048
    whole = [sizes[f] // P for f in looked]
    rest = [sizes[f] % P for f in looked]
    assert all(rest)
    chunks = [w + 1 for w in whole]
    max_chunks = max(chunks)
    widths = sorted(set(whole))
    RING = 8
    ROWS = 3
    PARTS = 3
    pieces = [[(0, 1), (1, w // 2), (w // 2, w)] if k == 0 else [(0, w)] for k, w in enumerate(whole)]

    def pieces_made(k):
        return sum(len(p) for p in pieces[:k + 1])

    last_chunk = [sum(chunks[:k + 1]) - 1 for k in range(LOOKUPS)]
    since = [LATE * P if k == LOOKUPS - 1 else 0 for k in range(LOOKUPS)]

    gathered = [f for f in range(n_tables) if f not in looked]
    PER = 4
    assert gathered[-1] == n_tables - 1
    order = [n_tables - 1, n_tables] + gathered[:-1] + [looked[-1]]
    n_lots = -(-len(order) // PER)
    assert (len(order) - 1) % PER > 0

    def lot(t, m):
        return [f for f in order[PER * m:PER * (m + 1)] if t < LATE or f != looked[-1]]

    HALF = 16
    HALVES = QUAD // HALF
    assert HALF * width <= 512

    ctx = ExitStack()
    with ctx:
        def sb(name, shape, dt=fp32):
            return ctx.enter_context(nc.sbuf_tensor(name, shape, dt))

        def pb(name, shape):
            return ctx.enter_context(nc.psum_tensor(name, shape, fp32))

        def sem(name):
            return ctx.enter_context(nc.semaphore(name))

        idx = sb("idx", [P, tiles, n_tables], i32)
        ids16 = sb("ids16", [P, tiles, n_tables], fp16)
        ident16 = sb("ident16", [P, P], fp16)
        table_rows = sb("table_rows", [P, ROWS, max_chunks, depth])
        table_hi = sb("table_hi", [P, PARTS, max_chunks, depth], fp32r)
        table_lo = sb("table_lo", [P, PARTS, max_chunks, depth], fp32r)
        row_of = [sb(f"row_of_{w}", [P, w]) for w in widths]
        minus_row = [sb(f"minus_row_{w}", [P, 1]) for w in widths]
        square = sb("square", [P, batch])
        one = sb("one", [P, 1])
        id_rows = sb("id_rows", [P, 2, batch])
        hot = sb("hot", [P, RING, batch], fp32r)
        rows = sb("rows", [P, tiles, len(order), depth])
        ident = sb("ident", [P, P])
        zero = sb("zero", [P, hid1])
        T = sb("T", [P, batch, slots])
        Z = sb("Z", [P, n_z, batch])
        W1z = sb("W1z", [P, n_z, hid1])
        W1x = sb("W1x", [P, hid1])
        W2 = sb("W2", [P, n1, hid2])
        n_small = n1 + n2 + n2
        small_rows = sb("small_rows", [n_small, P])
        small = sb("small", [P, n_small])
        B1 = small[:, 0:n1]
        B2 = small[:, n1:n1 + n2]
        W3 = small[:, n1 + n2:n_small]
        H1 = sb("H1", [P, n1, P])
        H2 = sb("H2", [P, n2, P])
        y = sb("y", [1, batch])

        pT = [pb(f"pT{i}", [P, PER * P]) for i in range(2)]
        pZ = [pb(f"pZ{i}", [P, HALVES, 512]) for i in range(2)]
        pH1 = pb("pH1", [P, n1 // 2, P])
        pH2 = pb("pH2", [P, n2 + 1, P])
        pY = pH2[0:1, n2, :]

        idx_in = sem("idx_in")
        dense_in = sem("dense_in")
        table_in = [sem(f"table_in_{i}") for i in range(ROWS)]
        ids16_made = sem("ids16_made")
        ids_spread = sem("ids_spread")
        ids_kept = sem("ids_kept")
        hi_made = sem("hi_made")
        lo_made = sem("lo_made")
        hot_made = sem("hot_made")
        squared = sem("squared")
        rest_hot_made = sem("rest_hot_made")
        one_set = sem("one_set")
        hot_used = sem("hot_used")
        looked_kept = sem("looked_kept")
        small_in = sem("small_in")
        small_turned = sem("small_turned")
        small_kept = sem("small_kept")
        w1_in = sem("w1_in")
        w2_in = sem("w2_in")
        rows_in = [[sem(f"rows_in_{t}_{m}") for m in range(n_lots)] for t in range(tiles)]
        ident_set = sem("ident_set")
        ident16_set = sem("ident16_set")
        row_of_set = sem("row_of_set")
        zero_set = sem("zero_set")
        pads_zero = sem("pads_zero")
        w1_zero = sem("w1_zero")
        lot_turned = sem("lot_turned")
        lot_kept_v = sem("lot_kept_v")
        lot_kept_a = sem("lot_kept_a")
        products = sem("products")
        beneath_v = sem("beneath_v")
        beneath_a = sem("beneath_a")
        spread_v = sem("spread_v")
        spread_a = sem("spread_a")
        h1_sum = sem("h1_sum")
        h1_kept = sem("h1_kept")
        h2_sum = sem("h2_sum")
        h2_kept = sem("h2_kept")
        h2_kept_a = sem("h2_kept_a")
        y_sum = sem("y_sum")
        y_kept = sem("y_kept")
        y_out = sem("y_out")

        UNITS = [range(0, n1 // 2), range(n1 // 2, n1)]

        def h1_psum(t, n):
            if t + 1 == tiles:
                return [pH1[:, 0, :], pT[1][:, 0:P], pZ[tiles % 2][:, 0, 0:P], pZ[tiles % 2][:, 1, 0:P]][n]
            if n in UNITS[0]:
                return pH1[:, n, :]
            k = (n - UNITS[1][0]) * P
            return pZ[(t + 1) % 2][:, HALVES - 1, k:k + P]

        def looked_psum(k):
            if since[k] > 0:
                return pH2[:, 0:(batch - since[k]) // P, :].rearrange("p n c -> p (n c)")
            return pZ[0][:, k % 2, :]

        def relu1_parts(t):
            return UNITS if t + 1 < tiles else [UNITS[0]] + [range(n, n + 1) for n in UNITS[1]]

        def h2_psum(t, n):
            return pH1[:, n - 1, :] if t + 1 == tiles and n > 0 else pH2[:, n, :]

        def y_psum(t):
            return pT[0][0:1, 0:P] if t + 1 == tiles else pY

        def lot_number(t, m):
            return t * n_lots + m

        def by_act(t, m):
            return t == 0 or m in (0, n_lots - 1)

        def wait_lot_kept(eng, t, m):
            before = [(u, k) for u in range(t + 1) for k in range(n_lots) if (u, k) <= (t, m)]
            count = sum(by_act(u, k) == by_act(t, m) for u, k in before)
            eng.wait_ge(lot_kept_a if by_act(t, m) else lot_kept_v, count)

        def lot_copies(t, m):
            fs = lot(t, m)
            starts = [s for s, f in enumerate(fs) if s == 0 or f != fs[s - 1] + 1]
            for s0, s1 in zip(starts, starts[1:] + [len(fs)]):
                src = pT[lot_number(t, m) % 2][:, s0 * P:s1 * P].rearrange("d (f b) -> d f b", f=s1 - s0)
                places = [DUPS + fs[s0]]
                if fs[s0] == feats - DUPS:
                    places.append(0)
                for f0 in places:
                    yield T[:, t * P:(t + 1) * P, f0:f0 + s1 - s0].rearrange("d b f -> d f b"), src

        def spread_copy(t, h, j, q):
            b0 = t * P + QUAD * j + HALF * h
            src = pZ[t % 2][QUAD * j:QUAD * j + slots, h, 0:HALF * width]
            src = src.rearrange("g (s i) -> g s i", i=width)[:, :, DUPS + first[q]:DUPS + first[q] + share[q]]
            return Z[QUAD * q:QUAD * q + slots, 0:share[q], b0:b0 + HALF].rearrange("g i s -> g s i"), src

        def overlay(t, h, j):
            b0 = t * P + QUAD * j + HALF * h
            src = pZ[t % 2][QUAD * j:QUAD * j + DUPS, h, 0:HALF * width]
            src = src.rearrange("g (s i) -> g s i", i=width)[:, :, DUPS + own:width]
            return Z[0:DUPS, 0:DUPS, b0:b0 + HALF].rearrange("g i s -> g s i"), src

        LOT_LAG = 1
        assert n_lots <= LOOKUPS - 1 - LOT_LAG
        LOTS = [range(0, 2), range(2, 3), range(3, n_lots)]
        AHEAD = 2
        LAST_LOTS = range(n_lots - 2, n_lots)

        def lots_in(t, part):
            if t == 1:
                return [range(AHEAD, 3), range(3, 4), range(4, n_lots)][part]
            return [m for m in LOTS[part] if t < tiles and not (t == tiles - 1 and m in LAST_LOTS)]

        QUADS_V = range(0, QUADS // 2)
        QUADS_A = range(QUADS // 2, QUADS)

        def load_table(k, queue):
            if k >= ROWS:
                queue.wait_ge(hi_made, pieces_made(k - ROWS))
                queue.wait_ge(lo_made, pieces_made(k - ROWS))
            table, w, n = tables[looked[k]], whole[k], whole[k] * P
            queue.dma_start(table_rows[:, k % ROWS, 0:w, :],
                            table[0:n, :].rearrange("(p c) d -> p c d", c=w)).then_inc(table_in[k % ROWS], 16)
            queue.dma_start(table_rows[0:rest[k], k % ROWS, w, :],
                            table[n:n + rest[k], :]).then_inc(table_in[k % ROWS], 16)

        block = ctx.enter_context(nc.Block())

        @block.sync
        def _(sp):
            sp.dma_start(idx[:, :, :], ids.rearrange("(t p) f -> p t f", p=P)).then_inc(idx_in, 16)

            def load_w1(i):
                q = max(q for q in range(QUADS) if first[q] <= i)
                sp.dma_start(W1z[QUAD * q + DUPS + i + 1:QUAD * q + slots, i - first[q], :],
                             w1[pair(i, i + 1):pair(i, feats), :]).then_inc(w1_in, 16)

            def load_w1_overlay(d):
                sp.dma_start(W1z[d:DUPS, d, :],
                             w1[pair(own + d, own + d + 1):pair(own + d, feats), :]).then_inc(w1_in, 16)

            sp.dma_start(small_rows[0:n1, :], b1.rearrange("(c p) -> c p", p=P)).then_inc(small_in, 16)
            sp.dma_start(small_rows[n1:n1 + n2, :], b2.rearrange("(c p) -> c p", p=P)).then_inc(small_in, 16)
            sp.dma_start(small_rows[n1 + n2:n_small, :],
                          w3.rearrange("(c p) o -> c (p o)", p=P)).then_inc(small_in, 16)
            for k in range(1, ROWS):
                load_table(k, sp)
            sp.dma_start(rows[:, :, order.index(n_tables), :],
                         dense.rearrange("(t p) d -> p t d", p=P)).then_inc(dense_in, 16)
            load_table(ROWS, sp)
            sp.wait_ge(zero_set, 1)
            sp.dma_start(W1z[:, :, :], zero[:, :].unsqueeze(1).broadcast_to((P, n_z, hid1))).then_inc(w1_zero, 16)
            for q in range(QUADS):
                sp.dma_start(Z[QUAD * q + slots:QUAD * (q + 1), :, :],
                             zero[0:QUAD - slots, :].unsqueeze(1).broadcast_to((QUAD - slots, n_z, batch))
                             ).then_inc(pads_zero, 16)
            W1_LOT = 4
            for k in range(ROWS + 1, LOOKUPS):
                load_table(k, sp)
                sp.wait_ge(w1_zero, 16)
                for i in range(W1_LOT * (k - ROWS - 1), W1_LOT * (k - ROWS)):
                    load_w1(i)
            for i in range(W1_LOT * (LOOKUPS - ROWS - 1), own):
                load_w1(i)
            for d in range(DUPS):
                load_w1_overlay(d)
            sp.dma_start(W1x[:, :], w1[n_pairs:n_pairs + depth, :]).then_inc(w2_in, 16)
            sp.dma_start(W2[:, :, :], w2.rearrange("(c p) n -> p c n", p=P)).then_inc(w2_in, 16)
            sp.wait_ge(y_kept, tiles)
            sp.dma_start(out.rearrange("b o -> o b"), y[:, :]).then_inc(y_out, 16)
            sp.wait_ge(y_out, 16)

        @block.gpsimd
        def _(pool):
            nc.gpsimd.memset(ident[:, :], 0.0).then_inc(ident_set, 1)
            pool.wait_ge(ident_set, 1)
            nc.gpsimd.affine_select(out=ident[:, :], in_=ident[:, :], compare_op=ALU.not_equal, fill=1.0,
                                    base=0, pattern=[[-1, P]], channel_multiplier=1).then_inc(ident_set, 1)
            for w, of, minus in zip(widths, row_of, minus_row):
                nc.gpsimd.iota(of[:, :], pattern=[[1, w]], base=0, channel_multiplier=w,
                               allow_small_or_imprecise_dtypes=True).then_inc(row_of_set, 1)
                nc.gpsimd.iota(minus[:, :], pattern=[[1, 1]], base=-w * P, channel_multiplier=-1,
                               allow_small_or_imprecise_dtypes=True).then_inc(row_of_set, 1)
            pool.wait_ge(idx_in, 16)
            for t in range(tiles):
                for m in range(n_lots):
                    for f in lot(t, m):
                        if f < n_tables:
                            pool.indirect_dma_start(
                                out=rows[:, t, order.index(f), :], out_offset=None, in_=tables[f],
                                in_offset=bass.IndirectOffsetOnAxis(ap=idx[:, t, f:f + 1], axis=0),
                            ).then_inc(rows_in[t][m], 16)

        @block.vector
        def _(dve):
            nc.vector.memset(zero[:, :], 0.0).then_inc(zero_set, 1)
            nc.vector.memset(one[:, :], 1.0).then_inc(one_set, 1)
            dve.wait_ge(ident_set, 2)
            nc.vector.tensor_copy(ident16[:, :], ident[:, :]).then_inc(ident16_set, 1)
            dve.wait_ge(idx_in, 16)
            nc.vector.tensor_copy(ids16[:, :, :], idx[:, :, :]).then_inc(ids16_made, 1)

            def make_lo(k, piece):
                dve.wait_ge(hi_made, pieces_made(k - 1) + piece + 1)
                if k >= PARTS:
                    dve.wait_ge(hot_used, last_chunk[k - PARTS] + 1)
                c0, c1 = pieces[k][piece]
                hi, lo = table_hi[:, k % PARTS], table_lo[:, k % PARTS]
                done = nc.vector.tensor_tensor(lo[:, c0:c1, :], table_rows[:, k % ROWS, c0:c1, :],
                                               hi[:, c0:c1, :], ALU.subtract)
                if c1 == whole[k]:
                    r = rest[k]
                    done = nc.vector.tensor_tensor(lo[0:r, c1, :], table_rows[0:r, k % ROWS, c1, :],
                                                   hi[0:r, c1, :], ALU.subtract)
                done.then_inc(lo_made, 1)

            def make_hot(k, some):
                dve.wait_ge(ids_kept, k + 1)
                if k == 0:
                    dve.wait_ge(row_of_set, 2 * len(widths))
                of = row_of[widths.index(whole[k])]
                for c in some:
                    n = sum(chunks[:k]) + c
                    if n >= RING:
                        dve.wait_ge(hot_used, n - RING + 1)
                    nc.vector.tensor_scalar(hot[:, n % RING, since[k]:], id_rows[:, k % 2, since[k]:], of[:, c:c + 1], None,
                                            ALU.is_equal).then_inc(hot_made, 1)

            def keep_lot(t, m):
                if not by_act(t, m):
                    dve.wait_ge(lot_turned, lot_number(t, m) + 1)
                    for to, of in lot_copies(t, m):
                        last = nc.vector.tensor_copy(to, of)
                    last.then_inc(lot_kept_v, 1)

            def spread(t, h):
                dve.wait_ge(products, HALVES * t + h + 1)
                for q in range(QUADS):
                    for j in QUADS_V:
                        last = nc.vector.tensor_copy(*spread_copy(t, h, j, q))
                        if q == 0:
                            last.then_inc(beneath_v, 1)
                dve.wait_ge(beneath_v, len(QUADS_V) * (HALVES * t + h + 1))
                for j in QUADS_V:
                    last = nc.vector.tensor_copy(*overlay(t, h, j))
                last.then_inc(spread_v, 1)

            def relu2(t):
                dve.wait_ge(h2_sum, t + 1)
                for n in range(n2 if t + 1 < tiles else 1):
                    last = nc.vector.tensor_scalar(H2[:, n, :], h2_psum(t, n), B2[:, n:n + 1], 0.0,
                                                   ALU.add, ALU.max)
                last.then_inc(h2_kept, 1)

            def keep_y(t):
                dve.wait_ge(y_sum, t + 1)
                nc.vector.tensor_copy(y[:, t * P:(t + 1) * P], y_psum(t)).then_inc(y_kept, 1)

            for k in range(LOOKUPS):
                if k == 0:
                    for piece in range(len(pieces[k])):
                        make_hot(k, range(piece, piece + 1))
                        make_lo(k, piece)
                    make_hot(k, range(len(pieces[k]), whole[k]))
                else:
                    make_lo(k, 0)
                    make_hot(k, range(whole[k]))
                if k == 1:
                    dve.wait_ge(small_turned, 1)
                    nc.vector.tensor_copy(small[:, :], pH2[:, 0, 0:n_small]).then_inc(small_kept, 1)
            for m in range(AHEAD):
                keep_lot(1, m)
            for t in range(tiles):
                for h in range(HALVES):
                    spread(t, h)
                for part in range(len(LOTS)):
                    for m in lots_in(t + 1, part):
                        keep_lot(t + 1, m)
                    if part == 0 and 0 < t < tiles - 1:
                        relu2(t - 1)
                    if part == 1 and t > 0:
                        keep_y(t - 1)
                if t + 2 == tiles:
                    for m in LAST_LOTS:
                        keep_lot(t + 1, m)
                    relu2(t)
            relu2(tiles - 1)
            keep_y(tiles - 1)

        @block.scalar
        def _(act):
            load_table(0, act)
            def keep_ids(k):
                act.wait_ge(ids_spread, k + 1)
                if k >= 2:
                    act.wait_ge(hot_made, sum(whole[:k - 1]))
                nc.scalar.copy(id_rows[:, k % 2, since[k]:], pZ[1][:, k % 2, since[k]:]).then_inc(ids_kept, 1)

            def make_hi(k):
                act.wait_ge(table_in[k % ROWS], 32 * (k // ROWS + 1))
                if k >= PARTS:
                    act.wait_ge(hot_used, last_chunk[k - PARTS] + 1)
                for c0, c1 in pieces[k]:
                    done = nc.scalar.copy(table_hi[:, k % PARTS, c0:c1, :], table_rows[:, k % ROWS, c0:c1, :])
                    if c1 == whole[k]:
                        done = nc.scalar.copy(table_hi[0:rest[k], k % PARTS, c1, :],
                                              table_rows[0:rest[k], k % ROWS, c1, :])
                    done.then_inc(hi_made, 1)

            def make_rest_hot(k):
                if k == 0:
                    act.wait_ge(row_of_set, 2 * len(widths))
                    act.wait_ge(one_set, 1)
                act.wait_ge(ids_kept, k + 1)
                nc.scalar.activation(square[:, since[k]:], id_rows[:, k % 2, since[k]:], ACT.Square,
                                     bias=minus_row[widths.index(whole[k])][:, :]).then_inc(squared, 1)
                n = last_chunk[k]
                if n >= RING:
                    act.wait_ge(hot_used, n - RING + 1)
                act.wait_ge(squared, k + 1)
                nc.scalar.activation(hot[:, n % RING, since[k]:], square[:, since[k]:], ACT.Relu,
                                     bias=one[:, :], scale=-2.0).then_inc(rest_hot_made, 1)

            def keep_looked(k):
                act.wait_ge(hot_used, last_chunk[k] + 1)
                nc.scalar.copy(T[:, since[k]:, DUPS + looked[k]], looked_psum(k)).then_inc(looked_kept, 1)

            def keep_lot(t, m):
                if by_act(t, m):
                    act.wait_ge(lot_turned, lot_number(t, m) + 1)
                    for to, of in lot_copies(t, m):
                        last = nc.scalar.copy(to, of)
                    last.then_inc(lot_kept_a, 1)

            def spread(t, h):
                act.wait_ge(products, HALVES * t + h + 1)
                for q in range(QUADS):
                    for j in QUADS_A:
                        last = nc.scalar.copy(*spread_copy(t, h, j, q))
                        if q == 0:
                            last.then_inc(beneath_a, 1)
                act.wait_ge(beneath_a, len(QUADS_A) * (HALVES * t + h + 1))
                for j in QUADS_A:
                    last = nc.scalar.copy(*overlay(t, h, j))
                last.then_inc(spread_a, 1)

            def relu1(t, part):
                act.wait_ge(h1_sum, len(UNITS) * t + part + 1)
                if t == 0 and part == 0:
                    act.wait_ge(small_kept, 1)
                for n in relu1_parts(t)[part]:
                    last = nc.scalar.activation(H1[:, n, :], h1_psum(t, n), ACT.Relu, bias=B1[:, n:n + 1])
                last.then_inc(h1_kept, 1)

            keep_ids(0)
            make_hi(0)
            make_rest_hot(0)
            keep_ids(1)
            make_hi(1)
            for k in range(LOOKUPS - 1):
                if k + 2 < LOOKUPS:
                    make_hi(k + 2)
                keep_looked(k)
                if k + 1 < LOOKUPS:
                    make_rest_hot(k + 1)
                if k + 2 < LOOKUPS:
                    keep_ids(k + 2)
                if 0 <= k - LOT_LAG < n_lots:
                    keep_lot(0, k - LOT_LAG)
            for m in range(AHEAD):
                keep_lot(1, m)
            for t in range(tiles):
                for h in range(HALVES):
                    spread(t, h)
                if t == 0:
                    keep_looked(LOOKUPS - 1)
                for part in range(len(LOTS)):
                    for m in lots_in(t + 1, part):
                        keep_lot(t + 1, m)
                    if part == 0:
                        relu1(t, 0)
                for part in range(1, len(relu1_parts(t))):
                    relu1(t, part)
                if t + 2 == tiles:
                    for m in LAST_LOTS:
                        keep_lot(t + 1, m)
            act.wait_ge(h2_sum, tiles + n2 - 1)
            for n in range(1, n2):
                last = nc.scalar.activation(H2[:, n, :], h2_psum(tiles - 1, n), ACT.Relu, bias=B2[:, n:n + 1])
            last.then_inc(h2_kept_a, 1)

        @block.tensor
        def _(pe):
            def turn_small():
                pe.wait_ge(ident_set, 2)
                pe.wait_ge(small_in, 48)
                nc.tensor.transpose(pH2[:, 0, 0:n_small], small_rows[:, :],
                                    ident[0:n_small, 0:n_small]).then_inc(small_turned, 1)

            def spread_ids(k):
                if k == 0:
                    pe.wait_ge(ids16_made, 1)
                    pe.wait_ge(ident16_set, 1)
                if k >= 2:
                    pe.wait_ge(ids_kept, k - 1)
                f = looked[k]
                for t in range(since[k] // P, tiles):
                    last = nc.tensor.matmul(pZ[1][:, k % 2, t * P:(t + 1) * P],
                                            ids16[:, t, f:f + 1].broadcast_to((P, P)), ident16[:, :],
                                            start=True, stop=True)
                last.then_inc(ids_spread, 1)

            def look_up(k):
                if k == LOOKUPS - 1:
                    pe.wait_ge(small_kept, 1)
                elif k >= 2:
                    pe.wait_ge(looked_kept, k - 1)
                for c in range(chunks[k]):
                    for piece, (c0, c1) in enumerate(pieces[k]):
                        if c == c0:
                            pe.wait_ge(lo_made, pieces_made(k - 1) + piece + 1)
                    n = sum(chunks[:k]) + c
                    r = P if c < whole[k] else rest[k]
                    if c < whole[k]:
                        pe.wait_ge(hot_made, sum(whole[:k]) + c + 1)
                    else:
                        pe.wait_ge(rest_hot_made, k + 1)
                    nc.tensor.matmul(looked_psum(k), table_hi[0:r, k % PARTS, c, :], hot[0:r, n % RING, since[k]:],
                                     start=c == 0, stop=False)
                    nc.tensor.matmul(looked_psum(k), table_lo[0:r, k % PARTS, c, :], hot[0:r, n % RING, since[k]:],
                                     start=False, stop=c == whole[k]).then_inc(hot_used, 1)

            def turn_lot(t, m):
                n = lot_number(t, m)
                if n >= 2:
                    wait_lot_kept(pe, (n - 2) // n_lots, (n - 2) % n_lots)
                if n_tables in lot(t, m) and t == 0:
                    pe.wait_ge(ident_set, 2)
                    pe.wait_ge(dense_in, 16)
                pe.wait_ge(rows_in[t][m], 16 * sum(f < n_tables for f in lot(t, m)))
                for s, f in enumerate(lot(t, m)):
                    last = nc.tensor.transpose(pT[n % 2][:, s * P:(s + 1) * P],
                                               rows[:, t, order.index(f), :], ident[:, :])
                last.then_inc(lot_turned, 1)

            def interact(t):
                if t == 0:
                    pe.wait_ge(looked_kept, LOOKUPS - 1)
                if t == LATE:
                    pe.wait_ge(looked_kept, LOOKUPS)
                if t >= 2:
                    pe.wait_ge(spread_v, HALVES * (t - 1))
                    pe.wait_ge(spread_a, HALVES * (t - 1))
                wait_lot_kept(pe, t, n_lots - 2)
                wait_lot_kept(pe, t, n_lots - 1)
                for s in range(QUAD):
                    if s == HALF and t > 0:
                        pe.wait_ge(h1_kept, 2 * t)
                    for j in range(QUADS):
                        b = t * P + QUAD * j + s
                        c0 = (s % HALF) * width
                        last = nc.tensor.matmul(
                            pZ[t % 2][QUAD * j:QUAD * j + slots, s // HALF, c0:c0 + width],
                            T[:, b, :], T[:, b, 0:width], start=True, stop=True)
                    if s % HALF == HALF - 1:
                        last.then_inc(products, 1)

            def layer1(t, n, x=True, z=True):
                if n == 0 and t == 0:
                    pe.wait_ge(w1_in, 16 * cols)
                    pe.wait_ge(w2_in, 32)
                    pe.wait_ge(pads_zero, 16 * QUADS)
                bs, ns = slice(t * P, (t + 1) * P), slice(n * P, (n + 1) * P)
                if x:
                    if n == 0 and t > 0:
                        pe.wait_ge(h1_kept, 2 * t)
                    nc.tensor.matmul(h1_psum(t, n), W1x[:, ns], T[:, bs, slots - 1], start=True, stop=False)
                if z:
                    if n == 0:
                        pe.wait_ge(spread_v, HALVES * (t + 1))
                        pe.wait_ge(spread_a, HALVES * (t + 1))
                    for c in range(n_z):
                        k = z_rows[c]
                        last = nc.tensor.matmul(h1_psum(t, n), W1z[0:k, c, ns], Z[0:k, c, bs],
                                                start=False, stop=c == n_z - 1)
                    if n in [part[-1] for part in relu1_parts(t)]:
                        last.then_inc(h1_sum, 1)

            def layer2(t, some=range(n1), units2=range(n2)):
                if 0 in some and 0 in units2:
                    if t == 0:
                        pe.wait_ge(looked_kept, LOOKUPS)
                    else:
                        pe.wait_ge(y_kept, t)
                steps = [(n, c) for n in units2 for c in some]
                if t + 1 == tiles:
                    steps = [(n, c) for c in some for n in units2]
                for n, c in steps:
                    for part, units in enumerate(relu1_parts(t)):
                        if n == 0 and c == units[0]:
                            pe.wait_ge(h1_kept, len(UNITS) * t + part + 1)
                    last = nc.tensor.matmul(h2_psum(t, n), W2[:, c, n * P:(n + 1) * P], H1[:, c, :],
                                            start=c == 0, stop=c == n1 - 1)
                    if c == n1 - 1 and (n == n2 - 1 or t + 1 == tiles):
                        last.then_inc(h2_sum, 1)

            def layer3(t):
                pe.wait_ge(h2_kept, t + 1)
                for c in range(n2):
                    if c == 1 and t + 1 == tiles:
                        pe.wait_ge(h2_kept_a, 1)
                    last = nc.tensor.matmul(y_psum(t), W3[:, c:c + 1], H2[:, c, :], start=c == 0, stop=c == n2 - 1)
                last.then_inc(y_sum, 1)

            spread_ids(0)
            turn_small()
            for k in range(LOOKUPS - 1):
                if k + 1 < LOOKUPS:
                    spread_ids(k + 1)
                look_up(k)
                if 0 <= k - LOT_LAG < n_lots:
                    turn_lot(0, k - LOT_LAG)
            for m in range(AHEAD):
                turn_lot(1, m)
            interact(0)
            look_up(LOOKUPS - 1)
            def turn_lots(t, part):
                for m in lots_in(t, part):
                    turn_lot(t, m)

            for t in range(tiles - 1):
                turn_lots(t + 1, 0)
                started = [UNITS[0][0], UNITS[1][0]] if t == 0 else []
                for n in started:
                    layer1(t, n, z=False)
                if t > 0:
                    layer2(t - 1)
                for n in range(n1):
                    layer1(t, n, x=n not in started)
                    if n in (1, 2):
                        turn_lots(t + 1, n)
                    if n == 1 and t > 0:
                        layer3(t - 1)
                if t + 2 == tiles:
                    for n, m in enumerate(LAST_LOTS):
                        turn_lot(t + 1, m)
                        layer2(t, units2=[n])
                interact(t + 1)
            t = tiles - 1
            layer3(t - 1)
            for n in range(n1):
                layer1(t, n, z=False)
            for n in range(n1):
                if n == n1 - 1:
                    layer2(t, UNITS[0])
                layer1(t, n, x=False)
            layer2(tiles - 1, UNITS[1])
            layer3(tiles - 1)


def kernel(**inputs):
    import numpy as np
    import concourse.bacc as bacc
    from concourse import mybir as mb
    from concourse.bass_utils import run_bass_kernel_spmd

    nc = bacc.Bacc("TRN2", target_bir_lowering=False, num_devices=1)
    arrays, aps = {}, {}
    for name, value in inputs.items():
        a = np.ascontiguousarray(value)
        arrays[f"in_{name}"] = a
        aps[name] = nc.dram_tensor(f"in_{name}", a.shape, mb.dt.from_np(a.dtype), kind="ExternalInput").ap()
    batch, n_tables = inputs["ids"].shape
    out = nc.dram_tensor("out", (batch, 1), mb.dt.float32, kind="ExternalOutput").ap()
    dlrm_tower(nc, aps["ids"], aps["r_dense_x"], [aps[f"tbl_{f}"] for f in range(n_tables)],
               aps["W_top1"], aps["b_top1"], aps["W_top2"], aps["b_top2"], aps["W_top3"], out)
    result = run_bass_kernel_spmd(nc, [arrays], core_ids=[0])
    return result.results[0]["out"]
```
